# Optimizing a Trainium2 kernel written in Bass

```python
import numpy as np
import jax
import jax.numpy as jnp

def _softmax(x, axis=-1):
    return jax.nn.softmax(x, axis=axis)

def _gelu(x):
    return jax.nn.gelu(x, approximate=True)

def _silu(x):
    return jax.nn.silu(x)

def _sigmoid(x):
    return jax.nn.sigmoid(x)

def _layernorm(x, axis=-1, eps=1e-05):
    m = jnp.mean(x, axis=axis, keepdims=True)
    v = jnp.var(x, axis=axis, keepdims=True)
    return (x - m) / jnp.sqrt(v + eps)

def _scatter_add(tgt, idx, src, axis=0):
    return tgt.at[idx].add(src)

def _segment_sum(src, seg, n):
    return jax.ops.segment_sum(src, seg, n)
kernel_name = 'mk_cond_resid_d2_seqx_r2_a05498'

def setup_inputs(seed: int=0):
    np.random.seed(seed)
    _w = jnp.asarray

    def _rec_inputs():
        import jax
        import jax.numpy as jnp
        _rk = jax.random.key(seed)
        x = -0.000125 + 0.9999 * jax.random.normal(jax.random.fold_in(_rk, 1), (32, 128, 512), jnp.float32)
        _lenS = 128 - jax.random.randint(jax.random.fold_in(_rk, 7), (32,), 0, max(1, 128 // 4) + 1, jnp.int32)
        _lenS2 = 128 - jax.random.randint(jax.random.fold_in(_rk, 8), (32,), 0, max(1, 128 // 4) + 1, jnp.int32)
        cond_1024 = -0.00493535 + 1.00056 * jax.random.normal(jax.random.fold_in(_rk, 11), (32, 512), jnp.float32)
        return (x, cond_1024)
    x, cond_1024 = _rec_inputs()

    def _L0_cond_setup():
        import jax, jax.numpy as jnp
        import numpy as np
        N, T, D, H = (64, 256, 512, 512)
        key = jax.random.key(seed)
        k1, k2, k3, k4 = jax.random.split(key, 4)
        x = jax.random.normal(k1, (N, T, D), dtype=jnp.float32)
        h0 = jax.random.normal(k2, (N, H), dtype=jnp.float32)
        Wx = jax.random.normal(k3, (D, H), dtype=jnp.float32) / np.sqrt(D)
        Wh = jax.random.normal(k4, (H, H), dtype=jnp.float32) / np.sqrt(H)
        b = jnp.zeros((H,), dtype=jnp.float32)
        return {'x': x, 'h0': h0, 'Wx': Wx, 'Wh': Wh, 'b': b}
    _L0_cond_all = _L0_cond_setup()
    _L0_cond_in = {k: v for k, v in _L0_cond_all.items() if k in ('Wx', 'Wh', 'b')}
    del _L0_cond_all

    def _L1_cond_setup():
        import jax, jax.numpy as jnp
        import numpy as np
        import math
        N, T, D, H = (64, 256, 512, 512)
        key = jax.random.key(seed)
        k1, k2, k3, k4 = jax.random.split(key, 4)
        x = jax.random.normal(k1, (N, T, D), dtype=jnp.float32)
        h0 = jax.random.normal(k2, (N, H), dtype=jnp.float32)
        Wx = jax.random.normal(k3, (D, 4 * H), dtype=jnp.float32) / math.sqrt(D)
        Wh = jax.random.normal(k4, (H, 4 * H), dtype=jnp.float32) / math.sqrt(H)
        b = jnp.zeros((4 * H,), dtype=jnp.float32)
        return {'x': x, 'h0': h0, 'Wx': Wx, 'Wh': Wh, 'b': b}
    _L1_cond_all = _L1_cond_setup()
    _L1_cond_in = {k: v for k, v in _L1_cond_all.items() if k in ('Wx', 'Wh', 'b')}
    del _L1_cond_all
    return {'x': x, 'cond_1024': cond_1024, 'L0_cond_Wx': _L0_cond_in['Wx'], 'L0_cond_Wh': _L0_cond_in['Wh'], 'L0_cond_b': _L0_cond_in['b'], 'L1_cond_Wx': _L1_cond_in['Wx'], 'L1_cond_Wh': _L1_cond_in['Wh'], 'L1_cond_b': _L1_cond_in['b']}

def reference(x, cond_1024, L0_cond_Wx, L0_cond_Wh, L0_cond_b, L1_cond_Wx, L1_cond_Wh, L1_cond_b):
    import jax
    import jax.numpy as jnp

    def _L0_cond_ref(x, h0, Wx, Wh, b):
        import jax, jax.numpy as jnp
        import numpy as np
        N, T, D, H = (64, 256, 512, 512)
        xW = jnp.einsum('ntd,dh->nth', x, Wx) + b
        xW_t = jnp.swapaxes(xW, 0, 1)

        def step(prev_h, xw):
            next_h = jnp.tanh(prev_h @ Wh + xw)
            return (next_h, next_h)
        _, h_t = jax.lax.scan(step, h0, xW_t)
        return jnp.swapaxes(h_t, 0, 1)

    def _L1_cond_ref(x, h0, Wx, Wh, b):
        import jax, jax.numpy as jnp
        import numpy as np
        import math
        N, T, D, H = (64, 256, 512, 512)
        Hdim = h0.shape[1]
        xW = jnp.einsum('ntd,dg->ntg', x, Wx) + b

        def step(carry, xw_t):
            prev_h, prev_c = carry
            a = xw_t + prev_h @ Wh
            i = jax.nn.sigmoid(a[:, :Hdim])
            f = jax.nn.sigmoid(a[:, Hdim:2 * Hdim])
            o = jax.nn.sigmoid(a[:, 2 * Hdim:3 * Hdim])
            g = jnp.tanh(a[:, 3 * Hdim:])
            next_c = f * prev_c + i * g
            next_h = o * jnp.tanh(next_c)
            return ((next_h, next_c), next_h)
        c0 = jnp.zeros_like(h0)
        _, hs = jax.lax.scan(step, (h0, c0), jnp.swapaxes(xW, 0, 1))
        return jnp.swapaxes(hs, 0, 1)
    x = x + _L0_cond_ref(x, cond_1024, L0_cond_Wx, L0_cond_Wh, L0_cond_b)
    x = x + _L1_cond_ref(x, cond_1024, L1_cond_Wx, L1_cond_Wh, L1_cond_b)
    return x

_drawn_inputs = setup_inputs


def setup_inputs(seed=0):
    import zlib

    import numpy as np

    out = dict(_drawn_inputs(seed))
    spreads = {'L0_cond_b': (0.0, 0.1), 'L1_cond_b': (0.0, 0.295)}
    factors = {}
    for name, (base, spread) in spreads.items():
        noise = np.random.default_rng([zlib.crc32(name.encode()), seed]).standard_normal(out[name].shape)
        drawn = base * np.exp(spread * noise) if base else spread * noise
        out[name] = jnp.asarray(drawn.astype(out[name].dtype))
    for name, factor in factors.items():
        out[name] = (out[name] * factor).astype(out[name].dtype)
    return out
```

```python
from contextlib import ExitStack

import concourse.bass as bass
from concourse import mybir

ALU = mybir.AluOpType
ACT = mybir.ActivationFunctionType
F32 = mybir.dt.float32
F32R = mybir.dt.float32r

P = 128
TG = 4
STAGES = 5
DMA = 16


def rnn_lstm_kernel(nc, x, h0, WxR, WhR, bR, WxL, WhL, bL, out):
    B, T, D = x.shape
    H = WhR.shape[0]
    J = H // P
    G = WhL.shape[1] // H
    GU = G * P
    NG = T // TG
    assert D == H and B * J == P and TG * B == P and J == TG and GU == 512

    ctx = ExitStack()
    with ctx:
        def sb(name, shape, dt=F32):
            return ctx.enter_context(nc.sbuf_tensor(name, shape, dt))

        def bank(name):
            return ctx.enter_context(nc.psum_tensor(name, [P, 512], F32))

        def sem(name):
            return ctx.enter_context(nc.semaphore(name))

        wxl_hi = sb("wxl_hi", [P, J, G * H], F32R)
        wxl_lo = sb("wxl_lo", [P, J, G * H], F32R)
        whl = sb("whl", [P, J, G * H])
        wxr_hi = sb("wxr_hi", [P, J, H], F32R)
        wxr_lo = sb("wxr_lo", [P, J, H], F32R)
        whr = sb("whr", [P, J, H])
        bias_l = sb("bias_l", [P, J, G, P])
        bias_r = sb("bias_r", [P, H])
        ident = sb("ident", [P, P])
        x_rows = sb("x_rows", [P, D])
        xT_hi = sb("xT_hi", [P, J, P], F32R)
        xT_lo = sb("xT_lo", [P, J, P], F32R)
        xT = sb("xT", [P, J, TG, B])
        yT = sb("yT", [P, J, TG, B])
        yT_hi = sb("yT_hi", [P, J, P], F32R)
        yT_lo = sb("yT_lo", [P, J, P], F32R)
        xr_sliced = sb("xr_sliced", [P, TG, P])
        xl_sliced = [sb("xl_sliced0", [P, TG, GU]), sb("xl_sliced1", [P, TG, GU])]
        x_sliced = sb("x_sliced", [P, TG, P])
        y_sliced = [sb("y_sliced0", [P, TG, P]), sb("y_sliced1", [P, TG, P])]
        result = sb("result", [P, TG, P])
        h0_sliced = sb("h0_sliced", [P, P])
        pre_r = sb("pre_r", [P, P])
        h_r = sb("h_r", [P, P])
        hT_r = sb("hT_r", [P, J, B])
        pre_l = sb("pre_l", [P, GU])
        gates = sb("gates", [P, GU])
        fc = sb("fc", [P, P])
        ig = sb("ig", [P, P])
        c = sb("c", [P, P])
        tanh_c = sb("tanh_c", [P, P])
        h_l = sb("h_l", [P, P])
        hT_l = sb("hT_l", [P, J, B])
        stage = xl_sliced

        ps_l = bank("ps_l")
        ps_r = bank("ps_r")
        ps_tr = bank("ps_tr")
        ps_tl = bank("ps_tl")
        ps_xt = bank("ps_xt")
        ps_xr = bank("ps_xr")
        ps_xl = [bank("ps_xl0"), bank("ps_xl1")]

        s_h0 = sem("h0_loaded")
        s_wxr = sem("wxr_loaded")
        s_whr = sem("whr_loaded")
        s_wxl = [sem("wxl_loaded0"), sem("wxl_loaded1")]
        s_whl = sem("whl_loaded")
        s_bias_r = sem("bias_r_loaded")
        s_bias_l = sem("bias_l_loaded")
        s_ident0 = sem("ident_zeroed")
        s_ident = sem("ident_ready")
        s_c0 = sem("c_zeroed")
        w_hi = sem("weights_high")
        w_split = sem("weights_split")
        x_rows_in = sem("x_rows_in")
        x_sliced_in = sem("x_sliced_in")
        x_T = sem("x_transposed")
        xT_high = sem("xT_high")
        xT_split = sem("xT_split")
        xT_whole = sem("xT_whole")
        xr_mm = sem("xr_product")
        xr_out = sem("xr_evacuated")
        rnn_mm = sem("rnn_product")
        rnn_pre = sem("rnn_preactivation")
        rnn_h = sem("rnn_h")
        rnn_T = sem("rnn_h_transposed")
        rnn_hT = sem("rnn_hT")
        y_done = sem("y_step")
        yT_done = sem("yT_step")
        yT_high = sem("yT_high")
        yT_split = sem("yT_split")
        xl_mm = sem("xl_product")
        xl_out = sem("xl_evacuated")
        lstm_mm = sem("lstm_product")
        lstm_pre = sem("lstm_preactivation")
        lstm_act = sem("lstm_activation")
        lstm_fc = sem("lstm_products_of_c")
        lstm_c = sem("lstm_c")
        lstm_h = sem("lstm_h")
        lstm_T = sem("lstm_h_transposed")
        lstm_hT = sem("lstm_hT")
        out_done = sem("out_step")
        stored = sem("out_stored")

        FIRST_FULL, LAST_FULL = STAGES, NG - 2

        def schedule(eng, step):
            for n in range(FIRST_FULL):
                step(n, n)
            assert (LAST_FULL + 1 - FIRST_FULL) % 2 == 0
            with eng.Fori(FIRST_FULL, LAST_FULL, 2) as n:
                step(n, FIRST_FULL)
                step(n + 1, FIRST_FULL + 1)
            for n in range(LAST_FULL + 1, NG + STAGES - 1):
                step(n, n)

        def works(at, stage_of):
            return 0 <= at - stage_of < NG

        def wait(eng, s, value):
            if not (isinstance(value, int) and value <= 0):
                eng.wait_ge(s, value)

        def sliced_dram(t, first):
            v = t.rearrange("b t (j u) -> j b t u", j=J)
            return [v[j, :, bass.ds(first, TG), :] for j in range(J)]

        block = ctx.enter_context(nc.Block())

        @block.sync
        def _(sp):
            def load_x_rows(group):
                src = x[:, bass.ds(group * TG, TG), :].rearrange("b t d -> t b d")
                sp.dma_start(x_rows[:, :], src).then_inc(x_rows_in, DMA)

            def load_x_sliced(group):
                for j, src in enumerate(sliced_dram(x, group * TG)):
                    sp.dma_start(x_sliced[j * B:(j + 1) * B, :, :], src).then_inc(x_sliced_in, DMA)

            def load_wxl(k):
                sp.dma_start(stage[(k + 1) % 2][:, :, :].rearrange("p a n -> p (a n)"),
                             WxL[k * P:(k + 1) * P, :]).then_inc(s_wxl[k % 2], DMA)

            def store(group):
                sp.wait_ge(out_done, TG * (group + 1))
                for j, dst in enumerate(sliced_dram(out, group * TG)):
                    sp.dma_start(dst, result[j * B:(j + 1) * B, :, :]).then_inc(stored, DMA)

            load_x_rows(0)
            for j in range(J):
                sp.dma_start(h0_sliced[j * B:(j + 1) * B, :], h0[:, j * P:(j + 1) * P]).then_inc(s_h0, DMA)
            sp.dma_start(stage[0][:, :, :], WxR.rearrange("(k p) n -> p k n", p=P)).then_inc(s_wxr, DMA)
            sp.dma_start(whr[:, :, :], WhR.rearrange("(k p) n -> p k n", p=P)).then_inc(s_whr, DMA)
            sp.dma_start(bias_r[:, :], bass.AP(tensor=bR.tensor, offset=0, ap=[[0, P], [1, H]])).then_inc(s_bias_r, DMA)
            for j in range(J):
                sp.dma_start(bias_l[:, j, :, :], bass.AP(tensor=bL.tensor, offset=j * P, ap=[[0, P], [H, G], [1, P]])
                             ).then_inc(s_bias_l, DMA)
            load_wxl(0)
            sp.wait_ge(w_split, 1)
            load_wxl(1)
            sp.dma_start(whl[:, :, :], WhL.rearrange("(k p) n -> p k n", p=P)).then_inc(s_whl, DMA)

            def body(n, at):
                if at == 2:
                    for k in (2, 3):
                        sp.wait_ge(w_split, k)
                        load_wxl(k)
                if works(at, 1):
                    wait(sp, y_done, (n - 1) * TG)
                    load_x_sliced(n - 1)
                if works(at, 4):
                    store(n - 4)
                if works(at + 1, 0):
                    sp.wait_ge(x_T, J * (n + 1))
                    load_x_rows(n + 1)

            schedule(sp, body)
            sp.wait_ge(stored, DMA * J * NG)

        def per_step(step):
            def body(n, at):
                for t in range(TG):
                    step(n, at, t)
            return body

        @block.gpsimd
        def _(pool):
            nc.gpsimd.memset(ident[:, :], 0.0).then_inc(s_ident0, 1)
            pool.wait_ge(s_ident0, 1)
            nc.gpsimd.affine_select(out=ident[:, :], in_=ident[:, :], compare_op=ALU.not_equal, fill=1.0, base=0,
                                    pattern=[[-1, P]], channel_multiplier=1).then_inc(s_ident, 1)

            def step(n, at, t):
                if works(at, 4):
                    s = (n - 4) * TG + t
                    if t == 0:
                        wait(pool, stored, DMA * J * (n - 4))
                    pool.wait_ge(lstm_h, s + 1)
                    nc.gpsimd.tensor_tensor(result[:, t, :], y_sliced[at % 2][:, t, :], h_l[:, :], ALU.add).then_inc(out_done, 1)
                if works(at, 2):
                    s = (n - 2) * TG + t
                    if t == 0:
                        pool.wait_ge(x_sliced_in, DMA * J * (n - 1))
                    if works(at, 4):
                        pool.wait_ge(out_done, (n - 4) * TG + t + 1)
                    pool.wait_ge(rnn_h, s + 1)
                    nc.gpsimd.tensor_tensor(y_sliced[at % 2][:, t, :], x_sliced[:, t, :], h_r[:, :], ALU.add).then_inc(y_done, 1)
                    if t == 0:
                        pool.wait_ge(xT_whole, n - 1)
                        wait(pool, yT_split, n - 2)
                    pool.wait_ge(rnn_hT, s + 2)
                    nc.gpsimd.tensor_tensor(yT[:, :, t, :], xT[:, :, t, :], hT_r[:, :, :], ALU.add).then_inc(yT_done, 1)
                if t == TG - 1:
                    if works(at, 1):
                        pool.wait_ge(xT_split, n)
                        if works(at, 2):
                            pool.wait_ge(yT_done, (n - 1) * TG)
                        nc.gpsimd.tensor_tensor(xT[:, :, :, :].rearrange("p k t b -> p (k t b)"),
                                                xT_hi[:, :, :].bitcast(F32).rearrange("p k m -> p (k m)"),
                                                xT_lo[:, :, :].bitcast(F32).rearrange("p k m -> p (k m)"),
                                                ALU.add).then_inc(xT_whole, 1)

            schedule(pool, per_step(step))

        @block.scalar
        def _(act):
            def split_high(loaded, value, src, dst):
                act.wait_ge(loaded, value)
                nc.scalar.activation(dst, src, ACT.Copy).then_inc(w_hi, 1)

            split_high(s_wxr, DMA, stage[0][:, :, :], wxr_hi[:, :, :])
            act.wait_ge(rnn_T, 1)
            nc.scalar.activation(hT_r[:, :, :].rearrange("p k b -> p (k b)"), ps_tr[:, 0:P], ACT.Copy).then_inc(rnn_hT, 1)

            def step(n, at, t):
                if works(at, 4):
                    s = (n - 4) * TG + t
                    act.wait_ge(lstm_pre, 2 * s + 1)
                    nc.scalar.activation(gates[:, 0:2 * P], pre_l[:, 0:2 * P], ACT.Sigmoid).then_inc(lstm_act, 1)
                    act.wait_ge(lstm_pre, 2 * s + 2)
                    nc.scalar.activation(gates[:, 3 * P:GU], pre_l[:, 3 * P:GU], ACT.Tanh).then_inc(lstm_act, 1)
                    nc.scalar.activation(gates[:, 2 * P:3 * P], pre_l[:, 2 * P:3 * P], ACT.Sigmoid).then_inc(lstm_act, 1)
                    act.wait_ge(lstm_c, s + 1)
                    nc.scalar.activation(tanh_c[:, :], c[:, :], ACT.Tanh).then_inc(lstm_act, 1)
                if works(at, 2):
                    s = (n - 2) * TG + t
                    act.wait_ge(rnn_pre, s + 1)
                    wait(act, y_done, s)
                    nc.scalar.activation(h_r[:, :], pre_r[:, :], ACT.Tanh).then_inc(rnn_h, 1)
                    act.wait_ge(rnn_T, s + 2)
                    wait(act, yT_done, s)
                    nc.scalar.activation(hT_r[:, :, :].rearrange("p k b -> p (k b)"), ps_tr[:, 0:P],
                                         ACT.Copy).then_inc(rnn_hT, 1)
                if at == 2:
                    split_high(s_wxl[t % 2], DMA * (t // 2 + 1), stage[(t + 1) % 2][:, :, :].rearrange("p a n -> p (a n)"),
                               wxl_hi[:, t, :])
                if t == TG - 1:
                    if works(at, 2):
                        act.wait_ge(yT_done, (n - 1) * TG)
                        if works(at, 3):
                            act.wait_ge(xl_mm, (n - 2) * J)
                        nc.scalar.activation(yT_hi[:, :, :].rearrange("p k m -> p (k m)"),
                                             yT[:, :, :, :].rearrange("p k t b -> p (k t b)"), ACT.Copy).then_inc(yT_high, 1)
                    if works(at, 0):
                        act.wait_ge(x_T, (n + 1) * J)
                        if works(at, 1):
                            act.wait_ge(xT_whole, n)
                        nc.scalar.activation(xT_hi[:, :, :].rearrange("p k m -> p (k m)"), ps_xt[:, :],
                                             ACT.Copy).then_inc(xT_high, 1)

            schedule(act, per_step(step))

        @block.vector
        def _(dve):
            nc.vector.memset(c[:, :], 0.0).then_inc(s_c0, 1)

            def split_low(src, high, dst):
                return nc.vector.tensor_tensor(dst, src, high.bitcast(F32), ALU.subtract)

            dve.wait_ge(w_hi, 1)
            split_low(stage[0][:, :, :], wxr_hi[:, :, :], wxr_lo[:, :, :]).then_inc(w_split, 1)
            dve.wait_ge(rnn_hT, 1)
            nc.vector.tensor_copy(hT_l[:, :, :], hT_r[:, :, :]).then_inc(lstm_hT, 1)
            dve.wait_ge(s_bias_r, DMA)
            dve.wait_ge(s_bias_l, DMA * J)

            def step(n, at, t):
                if works(at, 4):
                    s = (n - 4) * TG + t
                    if at == 4 and t == 0:
                        dve.wait_ge(s_c0, 1)
                    if t == 0:
                        dve.wait_ge(xl_out, J * (n - 3))
                    dve.wait_ge(lstm_mm, s + 1)
                    for half in (0, 1):
                        cols = slice(half * 2 * P, (half + 1) * 2 * P)
                        nc.vector.tensor_tensor(pre_l[:, cols], ps_l[:, cols], xl_sliced[at % 2][:, t, cols],
                                                ALU.add).then_inc(lstm_pre, 1)
                    dve.wait_ge(lstm_act, 4 * s + 1)
                    nc.vector.tensor_tensor(fc[:, :], gates[:, P:2 * P], c[:, :], ALU.mult).then_inc(lstm_fc, 1)
                    dve.wait_ge(lstm_act, 4 * s + 2)
                    nc.vector.tensor_tensor(ig[:, :], gates[:, 0:P], gates[:, 3 * P:GU], ALU.mult).then_inc(lstm_fc, 1)
                    dve.wait_ge(lstm_fc, 2 * s + 2)
                    nc.vector.tensor_tensor(c[:, :], fc[:, :], ig[:, :], ALU.add).then_inc(lstm_c, 1)
                if works(at, 2):
                    s = (n - 2) * TG + t
                    if t == 0:
                        dve.wait_ge(xr_out, n - 1)
                    dve.wait_ge(rnn_mm, s + 1)
                    nc.vector.tensor_tensor(pre_r[:, :], ps_r[:, 0:P], xr_sliced[:, t, :], ALU.add).then_inc(rnn_pre, 1)
                if works(at, 4):
                    s = (n - 4) * TG + t
                    dve.wait_ge(lstm_act, 4 * s + 4)
                    wait(dve, out_done, s)
                    nc.vector.tensor_tensor(h_l[:, :], gates[:, 2 * P:3 * P], tanh_c[:, :], ALU.mult).then_inc(lstm_h, 1)
                    dve.wait_ge(lstm_T, s + 1)
                    nc.vector.tensor_copy(hT_l[:, :, :].rearrange("p k b -> p (k b)"), ps_tl[:, 0:P]).then_inc(lstm_hT, 1)
                if works(at, 3):
                    dve.wait_ge(xl_mm, (n - 3) * J + t + 1)
                    for q in range(TG):
                        rows = slice(q * B, (q + 1) * B)
                        done = nc.vector.tensor_tensor(
                            xl_sliced[(at - 3) % 2][t * B:(t + 1) * B, q, :], ps_xl[t % 2][rows, :],
                            bias_l[rows, t, :, :].rearrange("p g u -> p (g u)"), ALU.add)
                    done.then_inc(xl_out, 1)
                if at == 2:
                    dve.wait_ge(w_hi, t + 2)
                    split_low(stage[(t + 1) % 2][:, :, :].rearrange("p a n -> p (a n)"), wxl_hi[:, t, :],
                              wxl_lo[:, t, :]).then_inc(w_split, 1)
                if t == TG - 1:
                    if works(at, 1):
                        dve.wait_ge(xr_mm, n)
                        for q in range(TG):
                            for j in range(J):
                                rows, cols = slice(q * B, (q + 1) * B), slice(j * P, (j + 1) * P)
                                done = nc.vector.tensor_tensor(xr_sliced[j * B:(j + 1) * B, q, :], ps_xr[rows, cols],
                                                               bias_r[rows, cols], ALU.add)
                        done.then_inc(xr_out, 1)
                    if works(at, 2):
                        dve.wait_ge(yT_high, n - 1)
                        split_low(yT[:, :, :, :].rearrange("p k t b -> p (k t b)"),
                                  yT_hi[:, :, :].rearrange("p k m -> p (k m)"),
                                  yT_lo[:, :, :].rearrange("p k m -> p (k m)")).then_inc(yT_split, 1)
                    if works(at, 0):
                        dve.wait_ge(xT_high, n + 1)
                        split_low(ps_xt[:, :], xT_hi[:, :, :].rearrange("p k m -> p (k m)"),
                                  xT_lo[:, :, :].rearrange("p k m -> p (k m)")).then_inc(xT_split, 1)

            schedule(dve, per_step(step))

        @block.tensor
        def _(pe):
            def recurrent(ps, hT, w, cols):
                for k in range(J):
                    for j in range(J):
                        last = nc.tensor.matmul(ps[j * B:(j + 1) * B, 0:cols], hT[:, k, :], w(k, j),
                                                start=(k == 0), stop=(k == J - 1))
                return last

            def whr_slice(k, j):
                return whr[:, k, j * P:(j + 1) * P]

            def whl_slice(k, j):
                return whl[:, k, :].rearrange("p (g j u) -> p j g u", j=J, u=P)[:, j, :, :]

            def wxl_slice(w, k, j):
                return w[:, k, :].rearrange("p (g j u) -> p j g u", j=J, u=P)[:, j, :, :]

            def input_product(ps, hi, lo, w_high, w_low, k):
                nc.tensor.matmul(ps[:, :], hi, w_high, start=(k == 0), stop=False)
                nc.tensor.matmul(ps[:, :], lo, w_high, start=False, stop=False)
                return nc.tensor.matmul(ps[:, :], hi, w_low, start=False, stop=(k == J - 1))

            pe.wait_ge(s_ident, 1)
            pe.wait_ge(s_h0, DMA * J)
            nc.tensor.transpose(ps_tr[:, 0:P], h0_sliced[:, :], ident[:, :]).then_inc(rnn_T, 1)

            def step(n, at, t):
                if works(at, 4):
                    s = (n - 4) * TG + t
                    if at == 4 and t == 0:
                        pe.wait_ge(s_whl, DMA)
                    pe.wait_ge(lstm_hT, s + 1)
                    recurrent(ps_l, hT_l, whl_slice, GU).then_inc(lstm_mm, 1)
                if works(at, 2):
                    s = (n - 2) * TG + t
                    if at == 2 and t == 0:
                        pe.wait_ge(s_whr, DMA)
                    pe.wait_ge(rnn_hT, s + 1)
                    recurrent(ps_r, hT_r, whr_slice, P).then_inc(rnn_mm, 1)
                if works(at, 3):
                    if at == 3 and t == 0:
                        pe.wait_ge(w_split, 1 + J)
                    if t == 0:
                        pe.wait_ge(yT_split, n - 2)
                    if at > 3 or t >= 2:
                        pe.wait_ge(xl_out, (n - 3) * J + t - 1)
                    for k in (0, 1):
                        input_product(ps_xl[t % 2], yT_hi[:, k, :], yT_lo[:, k, :],
                                      wxl_slice(wxl_hi, k, t), wxl_slice(wxl_lo, k, t), k)
                if works(at, 2):
                    pe.wait_ge(rnn_h, s + 1)
                    nc.tensor.transpose(ps_tr[:, 0:P], h_r[:, :], ident[:, :]).then_inc(rnn_T, 1)
                if works(at, 3):
                    for k in (2, 3):
                        last = input_product(ps_xl[t % 2], yT_hi[:, k, :], yT_lo[:, k, :],
                                             wxl_slice(wxl_hi, k, t), wxl_slice(wxl_lo, k, t), k)
                    last.then_inc(xl_mm, 1)
                if works(at, 4):
                    pe.wait_ge(lstm_h, (n - 4) * TG + t + 1)
                    nc.tensor.transpose(ps_tl[:, 0:P], h_l[:, :], ident[:, :]).then_inc(lstm_T, 1)
                if works(at, 1):
                    if at == 1 and t == 0:
                        pe.wait_ge(w_split, 1)
                    if t == 0:
                        pe.wait_ge(xT_split, n)
                        wait(pe, xr_out, n - 1)
                    last = input_product(ps_xr, xT_hi[:, t, :], xT_lo[:, t, :], wxr_hi[:, t, :], wxr_lo[:, t, :], t)
                    if t == TG - 1:
                        last.then_inc(xr_mm, 1)
                if works(at, 0):
                    if t == 0:
                        pe.wait_ge(x_rows_in, DMA * (n + 1))
                        wait(pe, xT_split, n)
                    nc.tensor.transpose(ps_xt[:, t * P:(t + 1) * P], x_rows[:, t * P:(t + 1) * P], ident[:, :]
                                        ).then_inc(x_T, 1)

            schedule(pe, per_step(step))


_INS = ["x", "cond_1024", "L0_cond_Wx", "L0_cond_Wh", "L0_cond_b", "L1_cond_Wx", "L1_cond_Wh", "L1_cond_b"]


def kernel(**inputs):
    import numpy as np
    import concourse.bacc as bacc
    from concourse.bass_utils import run_bass_kernel_spmd

    nc = bacc.Bacc("TRN2", target_bir_lowering=False, num_devices=1)
    arrays, args = {}, []
    for name in _INS:
        a = np.ascontiguousarray(inputs[name])
        arrays[f"in_{name}"] = a
        args.append(nc.dram_tensor(f"in_{name}", a.shape, mybir.dt.from_np(a.dtype), kind="ExternalInput").ap())
    shape = inputs["x"].shape
    out = nc.dram_tensor("out_0", shape, F32, kind="ExternalOutput").ap()
    rnn_lstm_kernel(nc, *args, out)
    r = run_bass_kernel_spmd(nc, [arrays], core_ids=[0])
    return r.results[0]["out_0"]
```

```python
from contextlib import ExitStack

import concourse.bass as bass
from concourse import mybir

ALU = mybir.AluOpType
ACT = mybir.ActivationFunctionType
F32 = mybir.dt.float32
F32R = mybir.dt.float32r

P = 128
TG = 4
STAGES = 5
DMA = 16


def rnn_lstm_kernel(nc, x, h0, WxR, WhR, bR, WxL, WhL, bL, out):
    B, T, D = x.shape
    H = WhR.shape[0]
    J = H // P
    G = WhL.shape[1] // H
    GU = G * P
    NG = T // TG
    assert D == H and B * J == P and TG * B == P and J == TG and GU == 512

    ctx = ExitStack()
    with ctx:
        def sb(name, shape, dt=F32):
            return ctx.enter_context(nc.sbuf_tensor(name, shape, dt))

        def bank(name):
            return ctx.enter_context(nc.psum_tensor(name, [P, 512], F32))

        def sem(name):
            return ctx.enter_context(nc.semaphore(name))

        wxl_hi = sb("wxl_hi", [P, J, G * H], F32R)
        wxl_lo = sb("wxl_lo", [P, J, G * H], F32R)
        whl = sb("whl", [P, J, G * H])
        wxr_hi = sb("wxr_hi", [P, J, H], F32R)
        wxr_lo = sb("wxr_lo", [P, J, H], F32R)
        whr = sb("whr", [P, J, H])
        bias_l = sb("bias_l", [P, J, G, P])
        bias_r = sb("bias_r", [P, H])
        ident = sb("ident", [P, P])
        x_rows = [sb("x_rows0", [P, D]), sb("x_rows1", [P, D])]
        xT_hi = sb("xT_hi", [P, J, P], F32R)
        xT_lo = sb("xT_lo", [P, J, P], F32R)
        xT = sb("xT", [P, J, TG, B])
        yT = sb("yT", [P, J, TG, B])
        yT_hi = sb("yT_hi", [P, J, P], F32R)
        yT_lo = sb("yT_lo", [P, J, P], F32R)
        xr_sliced = [sb("xr_sliced0", [P, TG, P]), sb("xr_sliced1", [P, TG, P])]
        xl_sliced = [sb("xl_sliced0", [P, TG, GU]), sb("xl_sliced1", [P, TG, GU])]
        x_sliced = sb("x_sliced", [P, TG, P])
        y_sliced = [sb("y_sliced0", [P, TG, P]), sb("y_sliced1", [P, TG, P])]
        result = sb("result", [P, TG, P])
        h0_sliced = sb("h0_sliced", [P, P])
        pre_r = sb("pre_r", [P, P])
        h_r = sb("h_r", [P, P])
        hT_r = sb("hT_r", [P, J, B])
        pre_l = sb("pre_l", [P, GU])
        gates = sb("gates", [P, GU])
        fc = sb("fc", [P, P])
        ig = sb("ig", [P, P])
        c = sb("c", [P, P])
        tanh_c = sb("tanh_c", [P, P])
        h_l = sb("h_l", [P, P])
        hT_l = sb("hT_l", [P, J, B])
        stage = xl_sliced + [sb("stage2", [P, TG, GU]), sb("stage3", [P, TG, GU])]
        WXR_STAGE, WXL_STAGE = 0, [1, 2, 3, 0]
        SPLIT_AT = {(1, 3): 0, (2, 0): 1, (2, 1): 2, (2, 2): 3}

        ps_l = bank("ps_l")
        ps_r = bank("ps_r")
        ps_tr = bank("ps_tr")
        ps_tl = bank("ps_tl")
        ps_xt = bank("ps_xt")
        ps_xr = bank("ps_xr")
        ps_xl = [bank("ps_xl0"), bank("ps_xl1")]

        s_h0 = sem("h0_loaded")
        s_wxr = sem("wxr_loaded")
        s_whr = sem("whr_loaded")
        s_wxl = [sem(f"wxl_loaded{k}") for k in range(J)]
        s_whl = sem("whl_loaded")
        s_bias_r = sem("bias_r_loaded")
        s_bias_l = sem("bias_l_loaded")
        s_ident0 = sem("ident_zeroed")
        s_ident = sem("ident_ready")
        s_c0 = sem("c_zeroed")
        w_hi = sem("weights_high")
        w_split = sem("weights_split")
        x_rows_in = [sem("x_rows_in0"), sem("x_rows_in1")]
        x_sliced_in = sem("x_sliced_in")
        x_T = sem("x_transposed")
        xT_high = sem("xT_high")
        xT_split = sem("xT_split")
        xT_whole = sem("xT_whole")
        xr_mm = sem("xr_product")
        xr_out = sem("xr_evacuated")
        rnn_mm = sem("rnn_product")
        rnn_pre = sem("rnn_preactivation")
        rnn_h = sem("rnn_h")
        rnn_T = sem("rnn_h_transposed")
        rnn_hT = sem("rnn_hT")
        y_done = sem("y_step")
        yT_done = sem("yT_step")
        yT_high = sem("yT_high")
        yT_split = sem("yT_split")
        xl_mm = sem("xl_product")
        xl_out = sem("xl_evacuated")
        lstm_mm = sem("lstm_product")
        lstm_pre = sem("lstm_preactivation")
        lstm_act = sem("lstm_activation")
        lstm_fc = sem("lstm_products_of_c")
        lstm_c = sem("lstm_c")
        lstm_h = sem("lstm_h")
        lstm_T = sem("lstm_h_transposed")
        lstm_hT = sem("lstm_hT")
        out_done = sem("out_step")
        stored = sem("out_stored")

        FIRST_FULL, LAST_FULL = STAGES, NG - 4

        def schedule(eng, step):
            for n in range(FIRST_FULL):
                step(n, n)
            assert (LAST_FULL + 1 - FIRST_FULL) % 2 == 0
            with eng.Fori(FIRST_FULL, LAST_FULL, 2) as n:
                step(n, FIRST_FULL)
                step(n + 1, FIRST_FULL + 1)
            for n in range(LAST_FULL + 1, NG + STAGES - 1):
                step(n, n)

        def works(at, stage_of):
            return 0 <= at - stage_of < NG

        def wait(eng, s, value):
            if not (isinstance(value, int) and value <= 0):
                eng.wait_ge(s, value)

        def sliced_dram(t, first):
            v = t.rearrange("b t (j u) -> j b t u", j=J)
            return [v[j, :, bass.ds(first, TG), :] for j in range(J)]

        def flat(t):
            return t[:, :, :].rearrange("p a n -> p (a n)")

        block = ctx.enter_context(nc.Block())

        @block.sync
        def _(sp):
            def load_x_rows(group, parity):
                src = x[:, bass.ds(group * TG, TG), :].rearrange("b t d -> t b d")
                sp.dma_start(x_rows[parity][:, :], src).then_inc(x_rows_in[parity], DMA)

            def load_x_sliced(group):
                for j, src in enumerate(sliced_dram(x, group * TG)):
                    sp.dma_start(x_sliced[j * B:(j + 1) * B, :, :], src).then_inc(x_sliced_in, DMA)

            def load_wxl(k):
                sp.dma_start(flat(stage[WXL_STAGE[k]]), WxL[k * P:(k + 1) * P, :]).then_inc(s_wxl[k], DMA)

            def load_whl(k):
                sp.dma_start(whl[:, k, :], WhL[k * P:(k + 1) * P, :]).then_inc(s_whl, DMA)

            def store(group):
                sp.wait_ge(out_done, TG * (group + 1))
                for j, dst in enumerate(sliced_dram(out, group * TG)):
                    sp.dma_start(dst, result[j * B:(j + 1) * B, :, :]).then_inc(stored, DMA)

            load_x_rows(0, 0)
            for j in range(J):
                sp.dma_start(h0_sliced[j * B:(j + 1) * B, :], h0[:, j * P:(j + 1) * P]).then_inc(s_h0, DMA)
            sp.dma_start(stage[WXR_STAGE][:, :, :], WxR.rearrange("(k p) n -> p k n", p=P)).then_inc(s_wxr, DMA)
            load_x_rows(1, 1)
            sp.dma_start(bias_r[:, :], bass.AP(tensor=bR.tensor, offset=0, ap=[[0, P], [1, H]])).then_inc(s_bias_r, DMA)
            sp.dma_start(whr[:, :, :], WhR.rearrange("(k p) n -> p k n", p=P)).then_inc(s_whr, DMA)
            load_x_sliced(0)
            for k in range(J - 1):
                load_wxl(k)
            sp.wait_ge(w_split, 1)
            load_wxl(J - 1)

            def body(n, at):
                if works(at, 1) and at > 1:
                    sp.wait_ge(y_done, (n - 1) * TG)
                    load_x_sliced(n - 1)
                if works(at, 4):
                    store(n - 4)
                if works(at + 2, 0):
                    sp.wait_ge(x_T, J * (n + 1))
                    load_x_rows(n + 2, at % 2)
                if at == 0:
                    for j in range(J):
                        sp.dma_start(bias_l[:, j, :, :], bass.AP(tensor=bL.tensor, offset=j * P,
                                                                 ap=[[0, P], [H, G], [1, P]])).then_inc(s_bias_l, DMA)
                    load_whl(0)
                    load_whl(1)
                if at == 1:
                    load_whl(2)
                    load_whl(3)

            schedule(sp, body)
            sp.wait_ge(stored, DMA * J * NG)

        def per_step(step):
            def body(n, at):
                for t in range(TG):
                    step(n, at, t)
            return body

        @block.gpsimd
        def _(pool):
            nc.gpsimd.memset(ident[:, :], 0.0).then_inc(s_ident0, 1)
            pool.wait_ge(s_ident0, 1)
            nc.gpsimd.affine_select(out=ident[:, :], in_=ident[:, :], compare_op=ALU.not_equal, fill=1.0, base=0,
                                    pattern=[[-1, P]], channel_multiplier=1).then_inc(s_ident, 1)

            def step(n, at, t):
                if works(at, 4):
                    s = (n - 4) * TG + t
                    if t == 0:
                        wait(pool, stored, DMA * J * (n - 4))
                    pool.wait_ge(lstm_h, s + 1)
                    nc.gpsimd.tensor_tensor(result[:, t, :], y_sliced[at % 2][:, t, :], h_l[:, :], ALU.add).then_inc(out_done, 1)
                if works(at, 2):
                    s = (n - 2) * TG + t
                    if t == 0:
                        pool.wait_ge(x_sliced_in, DMA * J * (n - 1))
                    if works(at, 4):
                        pool.wait_ge(out_done, (n - 4) * TG + t + 1)
                    pool.wait_ge(rnn_h, s + 1)
                    nc.gpsimd.tensor_tensor(y_sliced[at % 2][:, t, :], x_sliced[:, t, :], h_r[:, :], ALU.add).then_inc(y_done, 1)
                    if t == 0:
                        pool.wait_ge(xT_whole, n - 1)
                        wait(pool, yT_split, n - 2)
                    pool.wait_ge(rnn_hT, s + 2)
                    nc.gpsimd.tensor_tensor(yT[:, :, t, :], xT[:, :, t, :], hT_r[:, :, :], ALU.add).then_inc(yT_done, 1)
                if t == TG - 1:
                    if works(at, 1):
                        pool.wait_ge(xT_split, n)
                        if works(at, 2):
                            pool.wait_ge(yT_done, (n - 1) * TG)
                        nc.gpsimd.tensor_tensor(xT[:, :, :, :].rearrange("p k t b -> p (k t b)"),
                                                xT_hi[:, :, :].bitcast(F32).rearrange("p k m -> p (k m)"),
                                                xT_lo[:, :, :].bitcast(F32).rearrange("p k m -> p (k m)"),
                                                ALU.add).then_inc(xT_whole, 1)

            schedule(pool, per_step(step))

        @block.scalar
        def _(act):
            def split_high(loaded, src, dst):
                act.wait_ge(loaded, DMA)
                nc.scalar.activation(dst, src, ACT.Copy).then_inc(w_hi, 1)

            split_high(s_wxr, flat(stage[WXR_STAGE]), flat(wxr_hi))
            act.wait_ge(rnn_T, 1)
            nc.scalar.activation(hT_r[:, :, :].rearrange("p k b -> p (k b)"), ps_tr[:, 0:P], ACT.Copy).then_inc(rnn_hT, 1)

            def step(n, at, t):
                if works(at, 4):
                    s = (n - 4) * TG + t
                    act.wait_ge(lstm_pre, 2 * s + 1)
                    nc.scalar.activation(gates[:, 0:2 * P], pre_l[:, 0:2 * P], ACT.Sigmoid).then_inc(lstm_act, 1)
                    act.wait_ge(lstm_pre, 2 * s + 2)
                    nc.scalar.activation(gates[:, 3 * P:GU], pre_l[:, 3 * P:GU], ACT.Tanh).then_inc(lstm_act, 1)
                    nc.scalar.activation(gates[:, 2 * P:3 * P], pre_l[:, 2 * P:3 * P], ACT.Sigmoid).then_inc(lstm_act, 1)
                    act.wait_ge(lstm_c, s + 1)
                    nc.scalar.activation(tanh_c[:, :], c[:, :], ACT.Tanh).then_inc(lstm_act, 1)
                if works(at, 2):
                    s = (n - 2) * TG + t
                    act.wait_ge(rnn_pre, s + 1)
                    wait(act, y_done, s)
                    nc.scalar.activation(h_r[:, :], pre_r[:, :], ACT.Tanh).then_inc(rnn_h, 1)
                    act.wait_ge(rnn_T, s + 2)
                    wait(act, yT_done, s)
                    nc.scalar.activation(hT_r[:, :, :].rearrange("p k b -> p (k b)"), ps_tr[:, 0:P],
                                         ACT.Copy).then_inc(rnn_hT, 1)
                if (at, t) in SPLIT_AT:
                    k = SPLIT_AT[at, t]
                    split_high(s_wxl[k], flat(stage[WXL_STAGE[k]]), wxl_hi[:, k, :])
                if t == TG - 1:
                    if works(at, 2):
                        act.wait_ge(yT_done, (n - 1) * TG)
                        if works(at, 3):
                            act.wait_ge(xl_mm, (n - 2) * J)
                        nc.scalar.activation(yT_hi[:, :, :].rearrange("p k m -> p (k m)"),
                                             yT[:, :, :, :].rearrange("p k t b -> p (k t b)"), ACT.Copy).then_inc(yT_high, 1)
                    if works(at, 0):
                        act.wait_ge(x_T, (n + 1) * J)
                        if works(at, 1):
                            act.wait_ge(xT_whole, n)
                        nc.scalar.activation(xT_hi[:, :, :].rearrange("p k m -> p (k m)"), ps_xt[:, :],
                                             ACT.Copy).then_inc(xT_high, 1)

            schedule(act, per_step(step))

        @block.vector
        def _(dve):
            nc.vector.memset(c[:, :], 0.0).then_inc(s_c0, 1)

            def split_low(src, high, dst):
                return nc.vector.tensor_tensor(dst, src, high.bitcast(F32), ALU.subtract)

            dve.wait_ge(w_hi, 1)
            split_low(flat(stage[WXR_STAGE]), flat(wxr_hi), flat(wxr_lo)).then_inc(w_split, 1)
            dve.wait_ge(rnn_hT, 1)
            nc.vector.tensor_copy(hT_l[:, :, :], hT_r[:, :, :]).then_inc(lstm_hT, 1)

            def step(n, at, t):
                if works(at, 4):
                    s = (n - 4) * TG + t
                    if at == 4 and t == 0:
                        dve.wait_ge(s_c0, 1)
                    if t == 0:
                        dve.wait_ge(xl_out, J * (n - 3))
                    dve.wait_ge(lstm_mm, s + 1)
                    for half in (0, 1):
                        cols = slice(half * 2 * P, (half + 1) * 2 * P)
                        nc.vector.tensor_tensor(pre_l[:, cols], ps_l[:, cols], xl_sliced[at % 2][:, t, cols],
                                                ALU.add).then_inc(lstm_pre, 1)
                    dve.wait_ge(lstm_act, 4 * s + 1)
                    nc.vector.tensor_tensor(fc[:, :], gates[:, P:2 * P], c[:, :], ALU.mult).then_inc(lstm_fc, 1)
                    dve.wait_ge(lstm_act, 4 * s + 2)
                    nc.vector.tensor_tensor(ig[:, :], gates[:, 0:P], gates[:, 3 * P:GU], ALU.mult).then_inc(lstm_fc, 1)
                    dve.wait_ge(lstm_fc, 2 * s + 2)
                    nc.vector.tensor_tensor(c[:, :], fc[:, :], ig[:, :], ALU.add).then_inc(lstm_c, 1)
                if works(at, 2):
                    s = (n - 2) * TG + t
                    if t == 0:
                        dve.wait_ge(xr_out, 2 * (n - 1))
                    dve.wait_ge(rnn_mm, s + 1)
                    nc.vector.tensor_tensor(pre_r[:, :], ps_r[:, 0:P], xr_sliced[at % 2][:, t, :], ALU.add).then_inc(rnn_pre, 1)
                if works(at, 4):
                    s = (n - 4) * TG + t
                    dve.wait_ge(lstm_act, 4 * s + 4)
                    wait(dve, out_done, s)
                    nc.vector.tensor_tensor(h_l[:, :], gates[:, 2 * P:3 * P], tanh_c[:, :], ALU.mult).then_inc(lstm_h, 1)
                    dve.wait_ge(lstm_T, s + 1)
                    nc.vector.tensor_copy(hT_l[:, :, :].rearrange("p k b -> p (k b)"), ps_tl[:, 0:P]).then_inc(lstm_hT, 1)
                if works(at, 3):
                    if at == 3 and t == 0:
                        dve.wait_ge(s_bias_l, DMA * J)
                    dve.wait_ge(xl_mm, (n - 3) * J + t + 1)
                    for q in range(TG):
                        rows = slice(q * B, (q + 1) * B)
                        done = nc.vector.tensor_tensor(
                            xl_sliced[(at - 3) % 2][t * B:(t + 1) * B, q, :], ps_xl[t % 2][rows, :],
                            bias_l[rows, t, :, :].rearrange("p g u -> p (g u)"), ALU.add)
                    done.then_inc(xl_out, 1)
                if works(at, 1) and t % 2 == 0:
                    if at == 1 and t == 0:
                        dve.wait_ge(s_bias_r, DMA)
                    dve.wait_ge(xr_mm, (n - 1) * 2 + t // 2 + 1)
                    for j in (t, t + 1):
                        for q in range(TG):
                            rows, cols = slice(q * B, (q + 1) * B), slice(j * P, (j + 1) * P)
                            done = nc.vector.tensor_tensor(xr_sliced[(at - 1) % 2][j * B:(j + 1) * B, q, :],
                                                           ps_xr[rows, cols], bias_r[rows, cols], ALU.add)
                    done.then_inc(xr_out, 1)
                if (at, t) in SPLIT_AT:
                    k = SPLIT_AT[at, t]
                    dve.wait_ge(w_hi, k + 2)
                    split_low(flat(stage[WXL_STAGE[k]]), wxl_hi[:, k, :], wxl_lo[:, k, :]).then_inc(w_split, 1)
                if t == TG - 1:
                    if works(at, 2):
                        dve.wait_ge(yT_high, n - 1)
                        split_low(yT[:, :, :, :].rearrange("p k t b -> p (k t b)"),
                                  yT_hi[:, :, :].rearrange("p k m -> p (k m)"),
                                  yT_lo[:, :, :].rearrange("p k m -> p (k m)")).then_inc(yT_split, 1)
                    if works(at, 0):
                        dve.wait_ge(xT_high, n + 1)
                        split_low(ps_xt[:, :], xT_hi[:, :, :].rearrange("p k m -> p (k m)"),
                                  xT_lo[:, :, :].rearrange("p k m -> p (k m)")).then_inc(xT_split, 1)

            schedule(dve, per_step(step))

        @block.tensor
        def _(pe):
            def recurrent(ps, hT, w, cols):
                for k in range(J):
                    for j in range(J):
                        last = nc.tensor.matmul(ps[j * B:(j + 1) * B, 0:cols], hT[:, k, :], w(k, j),
                                                start=(k == 0), stop=(k == J - 1))
                return last

            def whr_slice(k, j):
                return whr[:, k, j * P:(j + 1) * P]

            def whl_slice(k, j):
                return whl[:, k, :].rearrange("p (g j u) -> p j g u", j=J, u=P)[:, j, :, :]

            def wxl_slice(w, k, j):
                return w[:, k, :].rearrange("p (g j u) -> p j g u", j=J, u=P)[:, j, :, :]

            def input_product(ps, hi, lo, w_high, w_low, k):
                nc.tensor.matmul(ps, hi, w_high, start=(k == 0), stop=False)
                nc.tensor.matmul(ps, lo, w_high, start=False, stop=False)
                return nc.tensor.matmul(ps, hi, w_low, start=False, stop=(k == J - 1))

            pe.wait_ge(s_ident, 1)
            pe.wait_ge(s_h0, DMA * J)
            nc.tensor.transpose(ps_tr[:, 0:P], h0_sliced[:, :], ident[:, :]).then_inc(rnn_T, 1)

            def step(n, at, t):
                if works(at, 4):
                    s = (n - 4) * TG + t
                    if at == 4 and t == 0:
                        pe.wait_ge(s_whl, DMA)
                    pe.wait_ge(lstm_hT, s + 1)
                    recurrent(ps_l, hT_l, whl_slice, GU).then_inc(lstm_mm, 1)
                if works(at, 2):
                    s = (n - 2) * TG + t
                    if at == 2 and t == 0:
                        pe.wait_ge(s_whr, DMA)
                    pe.wait_ge(rnn_hT, s + 1)
                    recurrent(ps_r, hT_r, whr_slice, P).then_inc(rnn_mm, 1)
                if works(at, 3):
                    if at == 3 and t == 0:
                        pe.wait_ge(w_split, 1 + J)
                    if t == 0:
                        pe.wait_ge(yT_split, n - 2)
                    if at > 3 or t >= 2:
                        pe.wait_ge(xl_out, (n - 3) * J + t - 1)
                    for k in (0, 1):
                        input_product(ps_xl[t % 2][:, :], yT_hi[:, k, :], yT_lo[:, k, :],
                                      wxl_slice(wxl_hi, k, t), wxl_slice(wxl_lo, k, t), k)
                if works(at, 2):
                    pe.wait_ge(rnn_h, s + 1)
                    nc.tensor.transpose(ps_tr[:, 0:P], h_r[:, :], ident[:, :]).then_inc(rnn_T, 1)
                if works(at, 3):
                    for k in (2, 3):
                        last = input_product(ps_xl[t % 2][:, :], yT_hi[:, k, :], yT_lo[:, k, :],
                                             wxl_slice(wxl_hi, k, t), wxl_slice(wxl_lo, k, t), k)
                    last.then_inc(xl_mm, 1)
                if works(at, 4):
                    pe.wait_ge(lstm_h, (n - 4) * TG + t + 1)
                    nc.tensor.transpose(ps_tl[:, 0:P], h_l[:, :], ident[:, :]).then_inc(lstm_T, 1)
                if works(at, 1) and t % 2 == 0:
                    if at == 1 and t == 0:
                        pe.wait_ge(w_split, 1)
                    if t == 0:
                        pe.wait_ge(xT_split, n)
                    wait(pe, xr_out, (n - 1) * 2 + t // 2)
                    cols = slice(t * P, (t + 2) * P)
                    for k in range(J):
                        last = input_product(ps_xr[:, cols], xT_hi[:, k, :], xT_lo[:, k, :],
                                             wxr_hi[:, k, cols], wxr_lo[:, k, cols], k)
                    last.then_inc(xr_mm, 1)
                if works(at, 0):
                    if t == 0:
                        pe.wait_ge(x_rows_in[at % 2], (n - at % 2 + 2) * (DMA // 2))
                        wait(pe, xT_split, n)
                    nc.tensor.transpose(ps_xt[:, t * P:(t + 1) * P], x_rows[at % 2][:, t * P:(t + 1) * P], ident[:, :]
                                        ).then_inc(x_T, 1)

            schedule(pe, per_step(step))


_INS = ["x", "cond_1024", "L0_cond_Wx", "L0_cond_Wh", "L0_cond_b", "L1_cond_Wx", "L1_cond_Wh", "L1_cond_b"]


def kernel(**inputs):
    import numpy as np
    import concourse.bacc as bacc
    from concourse.bass_utils import run_bass_kernel_spmd

    nc = bacc.Bacc("TRN2", target_bir_lowering=False, num_devices=1)
    arrays, args = {}, []
    for name in _INS:
        a = np.ascontiguousarray(inputs[name])
        arrays[f"in_{name}"] = a
        args.append(nc.dram_tensor(f"in_{name}", a.shape, mybir.dt.from_np(a.dtype), kind="ExternalInput").ap())
    shape = inputs["x"].shape
    out = nc.dram_tensor("out_0", shape, F32, kind="ExternalOutput").ap()
    rnn_lstm_kernel(nc, *args, out)
    r = run_bass_kernel_spmd(nc, [arrays], core_ids=[0])
    return r.results[0]["out_0"]
```

```python
from contextlib import ExitStack

import concourse.bass as bass
from concourse import mybir

ALU = mybir.AluOpType
ACT = mybir.ActivationFunctionType
F32 = mybir.dt.float32
F32R = mybir.dt.float32r
F16 = mybir.dt.float16
I32 = mybir.dt.int32

P = 128
TG = 4
STAGES = 5
DMA = 16
H_SCALE = 2.0 ** 14


def rnn_lstm_kernel(nc, x, h0, WxR, WhR, bR, WxL, WhL, bL, out):
    B, T, D = x.shape
    H = WhR.shape[0]
    J = H // P
    G = WhL.shape[1] // H
    GU = G * P
    NG = T // TG
    assert D == H and B * J == P and TG * B == P and J == TG and GU == 512

    ctx = ExitStack()
    with ctx:
        def sb(name, shape, dt=F32):
            return ctx.enter_context(nc.sbuf_tensor(name, shape, dt))

        def bank(name):
            return ctx.enter_context(nc.psum_tensor(name, [P, 512], F32))

        def sem(name):
            return ctx.enter_context(nc.semaphore(name))

        def flat(t):
            return t[:, :, :].rearrange("p a n -> p (a n)")

        wxl_hi = sb("wxl_hi", [P, J, G * H], F32R)
        wxl_lo = sb("wxl_lo", [P, J, G * H], F32R)
        whl = sb("whl", [P, J, G * H])
        wxr_hi = sb("wxr_hi", [P, J, H], F32R)
        wxr_lo = sb("wxr_lo", [P, J, H], F32R)
        whr = sb("whr", [P, J, H])
        bias_l = sb("bias_l", [P, J, G, P])
        bias_r = sb("bias_r", [P, H])
        ident = sb("ident", [P, P])
        x_rows = [sb("x_rows0", [P, D]), sb("x_rows1", [P, D])]
        xT_hi = sb("xT_hi", [P, J, P], F32R)
        xT_lo = sb("xT_lo", [P, J, P], F32R)
        xT = sb("xT", [P, J, TG, B])
        yT = sb("yT", [P, J, TG, B])
        yT_hi = sb("yT_hi", [P, J, P], F32R)
        yT_lo = sb("yT_lo", [P, J, P], F32R)
        xr_sliced = [sb("xr_sliced0", [P, TG, P]), sb("xr_sliced1", [P, TG, P])]
        xl_sliced = [sb("xl_sliced0", [P, TG, GU]), sb("xl_sliced1", [P, TG, GU])]
        x_sliced = sb("x_sliced", [P, TG, P])
        y_sliced = [sb("y_sliced0", [P, TG, P]), sb("y_sliced1", [P, TG, P])]
        result = sb("result", [P, TG, P])
        h0_sliced = sb("h0_sliced", [P, P])
        pre_r = sb("pre_r", [P, P])
        h_r = sb("h_r", [P, P])
        hT_r = sb("hT_r", [P, J, B])
        pre_l = sb("pre_l", [P, GU])
        gates = sb("gates", [P, GU])
        fc = sb("fc", [P, P])
        ig = sb("ig", [P, P])
        c = sb("c", [P, P])
        tanh_c = sb("tanh_c", [P, P])
        h_l = sb("h_l", [P, P])
        hT_hi = sb("hT_hi", [P, P], F16)
        hT_lo = sb("hT_lo", [P, P], F16)
        h0T = sb("h0T", [P, P])
        peaks = sb("peaks", [P, 8])
        peaks_all = sb("peaks_all", [P, 8])
        scales = sb("scales", [P, 16])
        peak, power, inverse, scale, unscale = (scales[:, 2 * i:2 * i + 2] for i in range(5))
        w_col, h0_col = slice(0, 1), slice(1, 2)
        stage = xl_sliced + [sb("stage2", [P, TG, GU]), sb("stage3", [P, TG, GU])]
        WXR_STAGE, WXL_STAGE = 0, [1, 2, 3, 0]
        WXR_HALVES = 2
        WXR_SECOND_AT = (1, 0)
        HIGH_AT = {(1, 1): 0, (1, 2): 1, (2, 0): 2, (2, 1): 3}
        LOW_AT = {(1, 2): 0, (2, 0): 1}
        LOW_ON_POOL = {(2, 0): 2, (2, 1): 2, (2, 2): 3, (2, 3): 3}
        MAX_AT = {(2, 1): [0], (2, 2): [1], (2, 3): [2, 3]}
        H0_AT = (3, 1)
        WHL_ORDER = [3, 2, 1, 0]
        WHL_HIGH_AT = {(3, 0): [0, 1], (3, 1): [2], (3, 2): [3]}
        WHL_LOW_AT = {(3, 1): 0, (3, 2): 2}
        WHL_LOW_ON_POOL = {(3, 1): 1, (3, 2): 3}
        whl_place = {3: flat(stage[3]), 2: flat(stage[2]), 1: whl[:, 3, :], 0: whl[:, 2, :]}

        def wxr_half(w, half):
            return w[:, :, half * H // 2:(half + 1) * H // 2]

        def whl_part(k, part):
            return whl_place[k].bitcast(F16)[:, part * G * H:(part + 1) * G * H]

        ps_l = bank("ps_l")
        ps_r = bank("ps_r")
        ps_tr = bank("ps_tr")
        ps_tl = bank("ps_tl")
        ps_xt = bank("ps_xt")
        ps_xr = bank("ps_xr")
        ps_xl = [bank("ps_xl0"), bank("ps_xl1")]

        s_h0 = sem("h0_loaded")
        s_wxr = sem("wxr_loaded")
        s_whr = sem("whr_loaded")
        s_wxl = [sem(f"wxl_loaded{k}") for k in range(J)]
        s_whl = [sem(f"whl_loaded{k}") for k in range(J)]
        s_bias_r = sem("bias_r_loaded")
        s_bias_l = sem("bias_l_loaded")
        s_ident0 = sem("ident_zeroed")
        s_ident = sem("ident_ready")
        s_c0 = sem("c_zeroed")
        w_hi = sem("weights_high")
        w_split = sem("weights_split")
        w_split_pool = sem("weights_split_pool")
        x_rows_in = [sem("x_rows_in0"), sem("x_rows_in1")]
        x_sliced_in = sem("x_sliced_in")
        x_T = sem("x_transposed")
        xT_high = sem("xT_high")
        xT_split = sem("xT_split")
        xT_whole = sem("xT_whole")
        xr_mm = sem("xr_product")
        xr_out = sem("xr_evacuated")
        rnn_mm = sem("rnn_product")
        rnn_pre = sem("rnn_preactivation")
        rnn_h = sem("rnn_h")
        rnn_T = sem("rnn_h_transposed")
        rnn_hT = sem("rnn_hT")
        y_done = sem("y_step")
        yT_done = sem("yT_step")
        yT_high = sem("yT_high")
        yT_split = sem("yT_split")
        xl_mm = sem("xl_product")
        xl_out = sem("xl_evacuated")
        lstm_mm = sem("lstm_product")
        lstm_pre = sem("lstm_preactivation")
        lstm_act = sem("lstm_activation")
        lstm_fc = sem("lstm_products_of_c")
        lstm_c = sem("lstm_c")
        lstm_h = sem("lstm_h")
        lstm_T = sem("lstm_h_transposed")
        lstm_hT_hi = sem("lstm_hT_high")
        lstm_hT_lo = sem("lstm_hT_low")
        h0T_kept = sem("h0T_kept")
        peak_sem = sem("peaks_taken")
        peaks_sem = sem("peaks_of_all_partitions")
        scale_sem = sem("scale_steps")
        whl_high = sem("whl_high")
        whl_scaled = sem("whl_scaled")
        whl_split = sem("whl_split")
        whl_split_pool = sem("whl_split_pool")
        out_done = sem("out_step")
        stored = sem("out_stored")

        SCALE_READY = 9

        FIRST_FULL, LAST_FULL = STAGES, NG - 4

        def schedule(eng, step):
            for n in range(FIRST_FULL):
                step(n, n)
            assert (LAST_FULL + 1 - FIRST_FULL) % 2 == 0
            with eng.Fori(FIRST_FULL, LAST_FULL, 2) as n:
                step(n, FIRST_FULL)
                step(n + 1, FIRST_FULL + 1)
            for n in range(LAST_FULL + 1, NG + STAGES - 1):
                step(n, n)

        def works(at, stage_of):
            return 0 <= at - stage_of < NG

        def wait(eng, s, value):
            if not (isinstance(value, int) and value <= 0):
                eng.wait_ge(s, value)

        def sliced_dram(t, first):
            v = t.rearrange("b t (j u) -> j b t u", j=J)
            return [v[j, :, bass.ds(first, TG), :] for j in range(J)]

        block = ctx.enter_context(nc.Block())

        @block.sync
        def _(sp):
            def load_x_rows(group, parity):
                src = x[:, bass.ds(group * TG, TG), :].rearrange("b t d -> t b d")
                sp.dma_start(x_rows[parity][:, :], src).then_inc(x_rows_in[parity], DMA)

            def load_x_sliced(group):
                for j, src in enumerate(sliced_dram(x, group * TG)):
                    sp.dma_start(x_sliced[j * B:(j + 1) * B, :, :], src).then_inc(x_sliced_in, DMA)

            def load_wxl(k):
                sp.dma_start(flat(stage[WXL_STAGE[k]]), WxL[k * P:(k + 1) * P, :]).then_inc(s_wxl[k], DMA)

            def load_whl(k):
                sp.dma_start(whl[:, k, :], WhL[k * P:(k + 1) * P, :]).then_inc(s_whl[k], DMA)

            def store(group):
                sp.wait_ge(out_done, TG * (group + 1))
                for j, dst in enumerate(sliced_dram(out, group * TG)):
                    sp.dma_start(dst, result[j * B:(j + 1) * B, :, :]).then_inc(stored, DMA)

            load_x_rows(0, 0)
            for j in range(J):
                sp.dma_start(h0_sliced[j * B:(j + 1) * B, :], h0[:, j * P:(j + 1) * P]).then_inc(s_h0, DMA)
            sp.dma_start(stage[WXR_STAGE][:, :, :], WxR.rearrange("(k p) n -> p k n", p=P)).then_inc(s_wxr, DMA)
            load_x_rows(1, 1)
            sp.dma_start(bias_r[:, :], bass.AP(tensor=bR.tensor, offset=0, ap=[[0, P], [1, H]])).then_inc(s_bias_r, DMA)
            sp.dma_start(whr[:, :, :], WhR.rearrange("(k p) n -> p k n", p=P)).then_inc(s_whr, DMA)
            load_x_sliced(0)
            for k in range(J - 1):
                load_wxl(k)
            sp.wait_ge(w_split, WXR_HALVES)
            load_wxl(J - 1)

            def body(n, at):
                if works(at, 1) and at > 1:
                    sp.wait_ge(y_done, (n - 1) * TG)
                    load_x_sliced(n - 1)
                if works(at, 4):
                    store(n - 4)
                if works(at + 2, 0):
                    sp.wait_ge(x_T, J * (n + 1))
                    load_x_rows(n + 2, at % 2)
                if at == 0:
                    for k in range(J):
                        load_whl(k)
                if at == 1:
                    for j in range(J):
                        sp.dma_start(bias_l[:, j, :, :], bass.AP(tensor=bL.tensor, offset=j * P,
                                                                 ap=[[0, P], [H, G], [1, P]])).then_inc(s_bias_l, DMA)

            schedule(sp, body)
            sp.wait_ge(stored, DMA * J * NG)

        def per_step(step):
            def body(n, at):
                for t in range(TG):
                    step(n, at, t)
            return body

        @block.gpsimd
        def _(pool):
            nc.gpsimd.memset(ident[:, :], 0.0).then_inc(s_ident0, 1)
            pool.wait_ge(s_ident0, 1)
            nc.gpsimd.affine_select(out=ident[:, :], in_=ident[:, :], compare_op=ALU.not_equal, fill=1.0, base=0,
                                    pattern=[[-1, P]], channel_multiplier=1).then_inc(s_ident, 1)

            def step(n, at, t):
                if works(at, 4):
                    s = (n - 4) * TG + t
                    if t == 0:
                        wait(pool, stored, DMA * J * (n - 4))
                    pool.wait_ge(lstm_h, s + 1)
                    nc.gpsimd.tensor_tensor(result[:, t, :], y_sliced[at % 2][:, t, :], h_l[:, :], ALU.add).then_inc(out_done, 1)
                if works(at, 2):
                    s = (n - 2) * TG + t
                    if t == 0:
                        pool.wait_ge(x_sliced_in, DMA * J * (n - 1))
                    if works(at, 4):
                        pool.wait_ge(out_done, (n - 4) * TG + t + 1)
                    pool.wait_ge(rnn_h, s + 1)
                    nc.gpsimd.tensor_tensor(y_sliced[at % 2][:, t, :], x_sliced[:, t, :], h_r[:, :], ALU.add).then_inc(y_done, 1)
                    if t == 0:
                        pool.wait_ge(xT_whole, n - 1)
                        wait(pool, yT_split, n - 2)
                    pool.wait_ge(rnn_hT, s + 2)
                    nc.gpsimd.tensor_tensor(yT[:, :, t, :], xT[:, :, t, :], hT_r[:, :, :], ALU.add).then_inc(yT_done, 1)
                if (at, t) in LOW_ON_POOL:
                    k = LOW_ON_POOL[at, t]
                    pool.wait_ge(w_hi, WXR_HALVES + k + 1)
                    for quarter in (0, 1) if t % 2 == 0 else (2, 3):
                        cols = slice(quarter * H, (quarter + 1) * H)
                        nc.gpsimd.tensor_tensor(wxl_lo[:, k, cols], flat(stage[WXL_STAGE[k]])[:, cols],
                                                wxl_hi[:, k, cols].bitcast(F32), ALU.subtract).then_inc(w_split_pool, 1)
                if (at, t) in WHL_LOW_ON_POOL:
                    i = WHL_LOW_ON_POOL[at, t]
                    pool.wait_ge(whl_high, i + 1)
                    nc.gpsimd.tensor_tensor(whl_part(WHL_ORDER[i], 1), whl[:, WHL_ORDER[i], :],
                                            whl_part(WHL_ORDER[i], 0), ALU.subtract).then_inc(whl_split_pool, 1)
                if at == 2 and t == TG - 1:
                    pool.wait_ge(peak_sem, J + 1)
                    nc.gpsimd.partition_all_reduce(peaks_all[:, 0:J + 1], peaks[:, 0:J + 1], P,
                                                   bass.bass_isa.ReduceOp.max).then_inc(peaks_sem, 1)
                if t == TG - 1:
                    if works(at, 1):
                        pool.wait_ge(xT_split, n)
                        if works(at, 2):
                            pool.wait_ge(yT_done, (n - 1) * TG)
                        nc.gpsimd.tensor_tensor(xT[:, :, :, :].rearrange("p k t b -> p (k t b)"),
                                                xT_hi[:, :, :].bitcast(F32).rearrange("p k m -> p (k m)"),
                                                xT_lo[:, :, :].bitcast(F32).rearrange("p k m -> p (k m)"),
                                                ALU.add).then_inc(xT_whole, 1)

            schedule(pool, per_step(step))

        @block.scalar
        def _(act):
            def split_high(loaded, src, dst):
                act.wait_ge(loaded, DMA)
                nc.scalar.activation(dst, src, ACT.Copy).then_inc(w_hi, 1)

            def split_wxr_high(half):
                split_high(s_wxr, *(wxr_half(w, half) for w in (stage[WXR_STAGE], wxr_hi)))

            split_wxr_high(0)
            act.wait_ge(rnn_T, 1)
            nc.scalar.activation(hT_r[:, :, :].rearrange("p k b -> p (k b)"), ps_tr[:, 0:P], ACT.Copy).then_inc(rnn_hT, 1)

            pool_tiles = list(WHL_LOW_ON_POOL.values())

            def step(n, at, t):
                if works(at, 4):
                    s = (n - 4) * TG + t
                    act.wait_ge(lstm_pre, 2 * s + 1)
                    nc.scalar.activation(gates[:, 0:2 * P], pre_l[:, 0:2 * P], ACT.Sigmoid).then_inc(lstm_act, 1)
                    act.wait_ge(lstm_pre, 2 * s + 2)
                    nc.scalar.activation(gates[:, 3 * P:GU], pre_l[:, 3 * P:GU], ACT.Tanh).then_inc(lstm_act, 1)
                    nc.scalar.activation(gates[:, 2 * P:3 * P], pre_l[:, 2 * P:3 * P], ACT.Sigmoid).then_inc(lstm_act, 1)
                    act.wait_ge(lstm_c, s + 1)
                    nc.scalar.activation(tanh_c[:, :], c[:, :], ACT.Tanh).then_inc(lstm_act, 1)
                if works(at, 2):
                    s = (n - 2) * TG + t
                    act.wait_ge(rnn_pre, s + 1)
                    wait(act, y_done, s)
                    nc.scalar.activation(h_r[:, :], pre_r[:, :], ACT.Tanh).then_inc(rnn_h, 1)
                    act.wait_ge(rnn_T, s + 2)
                    wait(act, yT_done, s)
                    nc.scalar.activation(hT_r[:, :, :].rearrange("p k b -> p (k b)"), ps_tr[:, 0:P],
                                         ACT.Copy).then_inc(rnn_hT, 1)
                if (at, t) == WXR_SECOND_AT:
                    split_wxr_high(1)
                if (at, t) in HIGH_AT:
                    k = HIGH_AT[at, t]
                    split_high(s_wxl[k], flat(stage[WXL_STAGE[k]]), wxl_hi[:, k, :])
                for i in WHL_HIGH_AT.get((at, t), []):
                    act.wait_ge(scale_sem, SCALE_READY)
                    k, factor = WHL_ORDER[i], scale[:, w_col]
                    if i in pool_tiles:
                        nc.scalar.activation(whl[:, k, :], whl[:, k, :], ACT.Copy, scale=factor).then_inc(whl_scaled, 1)
                        act.wait_ge(whl_scaled, pool_tiles.index(i) + 1)
                        factor = 1.0
                    if i >= 2:
                        if i - 2 in pool_tiles:
                            act.wait_ge(whl_split_pool, pool_tiles.index(i - 2) + 1)
                        else:
                            act.wait_ge(whl_split, list(WHL_LOW_AT.values()).index(i - 2) + 1)
                    nc.scalar.activation(whl_part(k, 0), whl[:, k, :], ACT.Copy, scale=factor).then_inc(whl_high, 1)
                if t == TG - 1:
                    if works(at, 2):
                        act.wait_ge(yT_done, (n - 1) * TG)
                        if works(at, 3):
                            act.wait_ge(xl_mm, (n - 2) * J)
                        nc.scalar.activation(yT_hi[:, :, :].rearrange("p k m -> p (k m)"),
                                             yT[:, :, :, :].rearrange("p k t b -> p (k t b)"), ACT.Copy).then_inc(yT_high, 1)
                    if works(at, 0):
                        act.wait_ge(x_T, (n + 1) * J)
                        if works(at, 1):
                            act.wait_ge(xT_whole, n)
                        nc.scalar.activation(xT_hi[:, :, :].rearrange("p k m -> p (k m)"), ps_xt[:, :],
                                             ACT.Copy).then_inc(xT_high, 1)

            schedule(act, per_step(step))

        @block.vector
        def _(dve):
            nc.vector.memset(c[:, :], 0.0).then_inc(s_c0, 1)

            def split_low(src, high, dst):
                return nc.vector.tensor_tensor(dst, src, high.bitcast(F32), ALU.subtract)

            def split_wxr_low(half):
                dve.wait_ge(w_hi, half + 1)
                split_low(*(wxr_half(w, half) for w in (stage[WXR_STAGE], wxr_hi, wxr_lo))).then_inc(w_split, 1)

            split_wxr_low(0)
            dve.wait_ge(s_h0, DMA * J)
            nc.vector.tensor_reduce(peaks[:, J:J + 1], h0_sliced[:, :], mybir.AxisListType.X, ALU.max,
                                    apply_absolute_value=True).then_inc(peak_sem, 1)
            dve.wait_ge(rnn_hT, 1)
            nc.vector.tensor_copy(h0T[:, :], hT_r[:, :, :].rearrange("p k b -> p (k b)")).then_inc(h0T_kept, 1)

            def find_scales():
                count = [0]

                def then(ins):
                    count[0] += 1
                    ins.then_inc(scale_sem, 1)
                    dve.wait_ge(scale_sem, count[0])

                dve.wait_ge(peaks_sem, 1)
                then(nc.vector.tensor_reduce(peak[:, w_col], peaks_all[:, 0:J], mybir.AxisListType.X, ALU.max))
                then(nc.vector.tensor_scalar(peak[:, w_col], peak[:, w_col], 2.0 ** -100, None, ALU.max))
                then(nc.vector.tensor_scalar(peak[:, h0_col], peaks_all[:, J:J + 1], 1.0, None, ALU.max))
                then(nc.vector.tensor_scalar(power.bitcast(I32), peak.bitcast(I32), 0x7F800000, None, ALU.bitwise_and))
                then(nc.vector.tensor_scalar(inverse[:, w_col], power[:, w_col], 2.0 ** -14, None, ALU.mult))
                then(nc.vector.tensor_scalar(inverse[:, h0_col], power[:, h0_col], 2.0 / H_SCALE, None, ALU.mult))
                then(nc.vector.reciprocal(scale, inverse))
                then(nc.vector.tensor_scalar(unscale[:, w_col], inverse[:, w_col], 1.0 / H_SCALE, None, ALU.mult))
                then(nc.vector.tensor_tensor(unscale[:, h0_col], inverse[:, w_col], inverse[:, h0_col], ALU.mult))
                assert count[0] == SCALE_READY

            def split_hT(src, factor):
                nc.vector.tensor_scalar(hT_hi[:, :], src, factor, None, ALU.mult).then_inc(lstm_hT_hi, 1)

            def split_hT_rest(src, factor):
                nc.vector.scalar_tensor_tensor(out=hT_lo[:, :], in0=src, scalar=factor, in1=hT_hi[:, :],
                                               op0=ALU.mult, op1=ALU.subtract).then_inc(lstm_hT_lo, 1)

            def prepare(at, t):
                if (at, t) == WXR_SECOND_AT:
                    split_wxr_low(1)
                if (at, t) in LOW_AT:
                    k = LOW_AT[at, t]
                    dve.wait_ge(w_hi, WXR_HALVES + k + 1)
                    split_low(flat(stage[WXL_STAGE[k]]), wxl_hi[:, k, :], wxl_lo[:, k, :]).then_inc(w_split, 1)
                for k in MAX_AT.get((at, t), []):
                    dve.wait_ge(s_whl[k], DMA)
                    nc.vector.tensor_reduce(peaks[:, k:k + 1], whl[:, k, :], mybir.AxisListType.X, ALU.max,
                                            apply_absolute_value=True).then_inc(peak_sem, 1)
                if at == 3 and t == 0:
                    find_scales()
                if (at, t) == H0_AT:
                    dve.wait_ge(h0T_kept, 1)
                    split_hT(h0T[:, :], scale[:, h0_col])
                    dve.wait_ge(lstm_hT_hi, 1)
                    split_hT_rest(h0T[:, :], scale[:, h0_col])
                if (at, t) in WHL_LOW_AT:
                    i = WHL_LOW_AT[at, t]
                    dve.wait_ge(whl_high, i + 1)
                    nc.vector.scalar_tensor_tensor(
                        out=whl_part(WHL_ORDER[i], 1), in0=whl[:, WHL_ORDER[i], :], scalar=scale[:, w_col],
                        in1=whl_part(WHL_ORDER[i], 0), op0=ALU.mult, op1=ALU.subtract).then_inc(whl_split, 1)

            def step(n, at, t):
                if works(at, 4):
                    s = (n - 4) * TG + t
                    first = at == 4 and t == 0
                    if first:
                        dve.wait_ge(s_c0, 1)
                    if t == 0:
                        dve.wait_ge(xl_out, J * (n - 3))
                    dve.wait_ge(lstm_mm, s + 1)
                    for half in (0, 1):
                        cols = slice(half * 2 * P, (half + 1) * 2 * P)
                        nc.vector.scalar_tensor_tensor(
                            out=pre_l[:, cols], in0=ps_l[:, cols], scalar=unscale[:, h0_col if first else w_col],
                            in1=xl_sliced[at % 2][:, t, cols], op0=ALU.mult, op1=ALU.add).then_inc(lstm_pre, 1)
                    dve.wait_ge(lstm_act, 4 * s + 1)
                    nc.vector.tensor_tensor(fc[:, :], gates[:, P:2 * P], c[:, :], ALU.mult).then_inc(lstm_fc, 1)
                    dve.wait_ge(lstm_act, 4 * s + 2)
                    nc.vector.tensor_tensor(ig[:, :], gates[:, 0:P], gates[:, 3 * P:GU], ALU.mult).then_inc(lstm_fc, 1)
                    dve.wait_ge(lstm_fc, 2 * s + 2)
                    nc.vector.tensor_tensor(c[:, :], fc[:, :], ig[:, :], ALU.add).then_inc(lstm_c, 1)
                if works(at, 2):
                    s = (n - 2) * TG + t
                    if t == 0:
                        dve.wait_ge(xr_out, 2 * (n - 1))
                    dve.wait_ge(rnn_mm, s + 1)
                    nc.vector.tensor_tensor(pre_r[:, :], ps_r[:, 0:P], xr_sliced[at % 2][:, t, :], ALU.add).then_inc(rnn_pre, 1)
                if at != 1 or t == 0:
                    prepare(at, t)
                if works(at, 4):
                    s = (n - 4) * TG + t
                    dve.wait_ge(lstm_act, 4 * s + 4)
                    wait(dve, out_done, s)
                    nc.vector.tensor_tensor(h_l[:, :], gates[:, 2 * P:3 * P], tanh_c[:, :], ALU.mult).then_inc(lstm_h, 1)
                    dve.wait_ge(lstm_T, s + 1)
                    split_hT(ps_tl[:, 0:P], H_SCALE)
                    dve.wait_ge(lstm_hT_hi, s + 2)
                    split_hT_rest(ps_tl[:, 0:P], H_SCALE)
                if works(at, 3):
                    if at == 3 and t == 0:
                        dve.wait_ge(s_bias_l, DMA * J)
                    dve.wait_ge(xl_mm, (n - 3) * J + t + 1)
                    for q in range(TG):
                        rows = slice(q * B, (q + 1) * B)
                        done = nc.vector.tensor_tensor(
                            xl_sliced[(at - 3) % 2][t * B:(t + 1) * B, q, :], ps_xl[t % 2][rows, :],
                            bias_l[rows, t, :, :].rearrange("p g u -> p (g u)"), ALU.add)
                    done.then_inc(xl_out, 1)
                if works(at, 1) and t % 2 == 0:
                    if at == 1 and t == 0:
                        dve.wait_ge(s_bias_r, DMA)
                    dve.wait_ge(xr_mm, (n - 1) * 2 + t // 2 + 1)
                    for j in (t, t + 1):
                        for q in range(TG):
                            rows, cols = slice(q * B, (q + 1) * B), slice(j * P, (j + 1) * P)
                            done = nc.vector.tensor_tensor(xr_sliced[(at - 1) % 2][j * B:(j + 1) * B, q, :],
                                                           ps_xr[rows, cols], bias_r[rows, cols], ALU.add)
                    done.then_inc(xr_out, 1)
                if at == 1 and t > 0:
                    prepare(at, t)
                if t == TG - 1:
                    if works(at, 2):
                        dve.wait_ge(yT_high, n - 1)
                        split_low(yT[:, :, :, :].rearrange("p k t b -> p (k t b)"),
                                  yT_hi[:, :, :].rearrange("p k m -> p (k m)"),
                                  yT_lo[:, :, :].rearrange("p k m -> p (k m)")).then_inc(yT_split, 1)
                    if works(at, 0):
                        dve.wait_ge(xT_high, n + 1)
                        split_low(ps_xt[:, :], xT_hi[:, :, :].rearrange("p k m -> p (k m)"),
                                  xT_lo[:, :, :].rearrange("p k m -> p (k m)")).then_inc(xT_split, 1)

            schedule(dve, per_step(step))

        @block.tensor
        def _(pe):
            def recurrent(ps, hT, w, cols):
                for k in range(J):
                    for j in range(J):
                        last = nc.tensor.matmul(ps[j * B:(j + 1) * B, 0:cols], hT[:, k, :], w(k, j),
                                                start=(k == 0), stop=(k == J - 1))
                return last

            def recurrent_split(low_count):
                for h_part, w_part in ((0, 0), (0, 1), (1, 0)):
                    if h_part == 1:
                        pe.wait_ge(lstm_hT_lo, low_count)
                    for k in range(J):
                        for j in range(J):
                            last = nc.tensor.matmul(
                                ps_l[j * B:(j + 1) * B, :], (hT_hi, hT_lo)[h_part][:, k * B:(k + 1) * B],
                                gate_slice(whl_part(k, w_part), j),
                                start=(h_part == w_part == 0 and k == 0), stop=(h_part == 1 and k == J - 1))
                return last

            def whr_slice(k, j):
                return whr[:, k, j * P:(j + 1) * P]

            def gate_slice(w, j):
                return w.rearrange("p (g j u) -> p j g u", j=J, u=P)[:, j, :, :]

            def input_product(ps, hi, lo, w_high, w_low, k):
                nc.tensor.matmul(ps, hi, w_high, start=(k == 0), stop=False)
                nc.tensor.matmul(ps, lo, w_high, start=False, stop=False)
                return nc.tensor.matmul(ps, hi, w_low, start=False, stop=(k == J - 1))

            def xl_tile(k, j):
                return input_product(ps_xl[j % 2][:, :], yT_hi[:, k, :], yT_lo[:, k, :],
                                     gate_slice(wxl_hi[:, k, :], j), gate_slice(wxl_lo[:, k, :], j), k)

            pe.wait_ge(s_ident, 1)
            pe.wait_ge(s_h0, DMA * J)
            nc.tensor.transpose(ps_tr[:, 0:P], h0_sliced[:, :], ident[:, :]).then_inc(rnn_T, 1)

            def step(n, at, t):
                if works(at, 4):
                    s = (n - 4) * TG + t
                    if at == 4 and t == 0:
                        pe.wait_ge(whl_split, len(WHL_LOW_AT))
                        pe.wait_ge(whl_split_pool, len(WHL_LOW_ON_POOL))
                    pe.wait_ge(lstm_hT_hi, s + 1)
                    recurrent_split(s + 1).then_inc(lstm_mm, 1)
                if works(at, 2):
                    s = (n - 2) * TG + t
                    if at == 2 and t == 0:
                        pe.wait_ge(s_whr, DMA)
                    pe.wait_ge(rnn_hT, s + 1)
                    recurrent(ps_r, hT_r, whr_slice, P).then_inc(rnn_mm, 1)
                if works(at, 3):
                    if at == 3 and t == 0:
                        pe.wait_ge(w_split, WXR_HALVES + len(LOW_AT))
                        pe.wait_ge(w_split_pool, 2 * len(LOW_ON_POOL))
                    if t == 0:
                        pe.wait_ge(yT_split, n - 2)
                    if at > 3 or t >= 2:
                        pe.wait_ge(xl_out, (n - 3) * J + t - 1)
                    for k in range(J - 1):
                        xl_tile(k, t)
                if works(at, 2):
                    pe.wait_ge(rnn_h, s + 1)
                    nc.tensor.transpose(ps_tr[:, 0:P], h_r[:, :], ident[:, :]).then_inc(rnn_T, 1)
                if works(at, 4):
                    pe.wait_ge(lstm_h, (n - 4) * TG + t + 1)
                    nc.tensor.transpose(ps_tl[:, 0:P], h_l[:, :], ident[:, :]).then_inc(lstm_T, 1)
                if works(at, 3):
                    xl_tile(3, t).then_inc(xl_mm, 1)
                if works(at, 1) and t % 2 == 0:
                    if at == 1:
                        pe.wait_ge(w_split, t // 2 + 1)
                    if t == 0:
                        pe.wait_ge(xT_split, n)
                    wait(pe, xr_out, (n - 1) * 2 + t // 2)
                    cols = slice(t * P, (t + 2) * P)
                    for k in range(J):
                        last = input_product(ps_xr[:, cols], xT_hi[:, k, :], xT_lo[:, k, :],
                                             wxr_hi[:, k, cols], wxr_lo[:, k, cols], k)
                    last.then_inc(xr_mm, 1)
                if works(at, 0):
                    if t == 0:
                        pe.wait_ge(x_rows_in[at % 2], (n - at % 2 + 2) * (DMA // 2))
                        wait(pe, xT_split, n)
                    nc.tensor.transpose(ps_xt[:, t * P:(t + 1) * P], x_rows[at % 2][:, t * P:(t + 1) * P], ident[:, :]
                                        ).then_inc(x_T, 1)

            schedule(pe, per_step(step))


_INS = ["x", "cond_1024", "L0_cond_Wx", "L0_cond_Wh", "L0_cond_b", "L1_cond_Wx", "L1_cond_Wh", "L1_cond_b"]


def kernel(**inputs):
    import numpy as np
    import concourse.bacc as bacc
    from concourse.bass_utils import run_bass_kernel_spmd

    nc = bacc.Bacc("TRN2", target_bir_lowering=False, num_devices=1)
    arrays, args = {}, []
    for name in _INS:
        a = np.ascontiguousarray(inputs[name])
        arrays[f"in_{name}"] = a
        args.append(nc.dram_tensor(f"in_{name}", a.shape, mybir.dt.from_np(a.dtype), kind="ExternalInput").ap())
    shape = inputs["x"].shape
    out = nc.dram_tensor("out_0", shape, F32, kind="ExternalOutput").ap()
    rnn_lstm_kernel(nc, *args, out)
    r = run_bass_kernel_spmd(nc, [arrays], core_ids=[0])
    return r.results[0]["out_0"]
```
